# Optimizing a Trainium2 kernel written in Bass

```python
import numpy as np
import jax
import jax.numpy as jnp

def _softmax(x, axis=-1):
    return jax.nn.softmax(x, axis=axis)

def _gelu(x):
    return jax.nn.gelu(x, approximate=True)

def _silu(x):
    return jax.nn.silu(x)

def _sigmoid(x):
    return jax.nn.sigmoid(x)

def _layernorm(x, axis=-1, eps=1e-05):
    m = jnp.mean(x, axis=axis, keepdims=True)
    v = jnp.var(x, axis=axis, keepdims=True)
    return (x - m) / jnp.sqrt(v + eps)

def _scatter_add(tgt, idx, src, axis=0):
    return tgt.at[idx].add(src)

def _segment_sum(src, seg, n):
    return jax.ops.segment_sum(src, seg, n)
kernel_name = 'mk_dlrm_tower_d1_rec_r8_5a15b2'

def setup_inputs(seed: int=0):
    np.random.seed(seed)
    _w = jnp.asarray

    def _rec_inputs():
        import jax
        import jax.numpy as jnp
        _tk = jax.random.key(seed)
        dense_ctx = jax.random.normal(jax.random.fold_in(_tk, 190), (2048, 16), jnp.float32)
        ids = jnp.stack([jax.random.randint(jax.random.fold_in(_tk, 200 + f), (2048,), 0, v, jnp.int32) for f, v in enumerate([12500, 12500, 12500, 1000, 125000, 1250, 1250, 12500, 12500, 1000, 1000, 1250, 1000, 12500, 12500, 1000, 1250, 12500, 1000, 1250, 1000, 1000, 1000, 1000, 1000, 1000, 1000])], axis=1)
        tbl_0 = 0.05 * jax.random.normal(jax.random.fold_in(_tk, 500 + 0), (12500, 128), jnp.float32)
        tbl_1 = 0.05 * jax.random.normal(jax.random.fold_in(_tk, 500 + 1), (12500, 128), jnp.float32)
        tbl_2 = 0.05 * jax.random.normal(jax.random.fold_in(_tk, 500 + 2), (12500, 128), jnp.float32)
        tbl_3 = 0.05 * jax.random.normal(jax.random.fold_in(_tk, 500 + 3), (1000, 128), jnp.float32)
        tbl_4 = 0.05 * jax.random.normal(jax.random.fold_in(_tk, 500 + 4), (125000, 128), jnp.float32)
        tbl_5 = 0.05 * jax.random.normal(jax.random.fold_in(_tk, 500 + 5), (1250, 128), jnp.float32)
        tbl_6 = 0.05 * jax.random.normal(jax.random.fold_in(_tk, 500 + 6), (1250, 128), jnp.float32)
        tbl_7 = 0.05 * jax.random.normal(jax.random.fold_in(_tk, 500 + 7), (12500, 128), jnp.float32)
        tbl_8 = 0.05 * jax.random.normal(jax.random.fold_in(_tk, 500 + 8), (12500, 128), jnp.float32)
        tbl_9 = 0.05 * jax.random.normal(jax.random.fold_in(_tk, 500 + 9), (1000, 128), jnp.float32)
        tbl_10 = 0.05 * jax.random.normal(jax.random.fold_in(_tk, 500 + 10), (1000, 128), jnp.float32)
        tbl_11 = 0.05 * jax.random.normal(jax.random.fold_in(_tk, 500 + 11), (1250, 128), jnp.float32)
        tbl_12 = 0.05 * jax.random.normal(jax.random.fold_in(_tk, 500 + 12), (1000, 128), jnp.float32)
        tbl_13 = 0.05 * jax.random.normal(jax.random.fold_in(_tk, 500 + 13), (12500, 128), jnp.float32)
        tbl_14 = 0.05 * jax.random.normal(jax.random.fold_in(_tk, 500 + 14), (12500, 128), jnp.float32)
        tbl_15 = 0.05 * jax.random.normal(jax.random.fold_in(_tk, 500 + 15), (1000, 128), jnp.float32)
        tbl_16 = 0.05 * jax.random.normal(jax.random.fold_in(_tk, 500 + 16), (1250, 128), jnp.float32)
        tbl_17 = 0.05 * jax.random.normal(jax.random.fold_in(_tk, 500 + 17), (12500, 128), jnp.float32)
        tbl_18 = 0.05 * jax.random.normal(jax.random.fold_in(_tk, 500 + 18), (1000, 128), jnp.float32)
        tbl_19 = 0.05 * jax.random.normal(jax.random.fold_in(_tk, 500 + 19), (1250, 128), jnp.float32)
        tbl_20 = 0.05 * jax.random.normal(jax.random.fold_in(_tk, 500 + 20), (1000, 128), jnp.float32)
        tbl_21 = 0.05 * jax.random.normal(jax.random.fold_in(_tk, 500 + 21), (1000, 128), jnp.float32)
        tbl_22 = 0.05 * jax.random.normal(jax.random.fold_in(_tk, 500 + 22), (1000, 128), jnp.float32)
        tbl_23 = 0.05 * jax.random.normal(jax.random.fold_in(_tk, 500 + 23), (1000, 128), jnp.float32)
        tbl_24 = 0.05 * jax.random.normal(jax.random.fold_in(_tk, 500 + 24), (1000, 128), jnp.float32)
        tbl_25 = 0.05 * jax.random.normal(jax.random.fold_in(_tk, 500 + 25), (1000, 128), jnp.float32)
        tbl_26 = 0.05 * jax.random.normal(jax.random.fold_in(_tk, 500 + 26), (1000, 128), jnp.float32)
        _rk = jax.random.fold_in(_tk, 7)
        W_top1 = 0.0521996 * jax.random.normal(jax.random.fold_in(_tk, 801), (367, 512), jnp.float32)
        W_top2 = 0.0441942 * jax.random.normal(jax.random.fold_in(_tk, 802), (512, 256), jnp.float32)
        W_top3 = 0.0625 * jax.random.normal(jax.random.fold_in(_tk, 803), (256, 1), jnp.float32)
        b_top1 = jnp.zeros((512,), jnp.float32)
        b_top2 = jnp.zeros((256,), jnp.float32)
        return (dense_ctx, ids, tbl_0, tbl_1, tbl_2, tbl_3, tbl_4, tbl_5, tbl_6, tbl_7, tbl_8, tbl_9, tbl_10, tbl_11, tbl_12, tbl_13, tbl_14, tbl_15, tbl_16, tbl_17, tbl_18, tbl_19, tbl_20, tbl_21, tbl_22, tbl_23, tbl_24, tbl_25, tbl_26, W_top1, b_top1, W_top2, b_top2, W_top3)
    dense_ctx, ids, tbl_0, tbl_1, tbl_2, tbl_3, tbl_4, tbl_5, tbl_6, tbl_7, tbl_8, tbl_9, tbl_10, tbl_11, tbl_12, tbl_13, tbl_14, tbl_15, tbl_16, tbl_17, tbl_18, tbl_19, tbl_20, tbl_21, tbl_22, tbl_23, tbl_24, tbl_25, tbl_26, W_top1, b_top1, W_top2, b_top2, W_top3 = _rec_inputs()

    def _L0_rec_setup():
        import jax, jax.numpy as jnp
        import numpy as np
        NUM_FEATURES = 27
        EMBED_DIM = 128
        BATCH = 4096
        key = jax.random.key(seed)
        inputs = jax.random.normal(key, (BATCH, NUM_FEATURES, EMBED_DIM), dtype=jnp.float32)
        return {'inputs': inputs}
    _L0_rec_all = _L0_rec_setup()
    _L0_rec_in = {k: v for k, v in _L0_rec_all.items() if k in ()}
    del _L0_rec_all
    return {'dense_ctx': dense_ctx, 'ids': ids, 'tbl_0': tbl_0, 'tbl_1': tbl_1, 'tbl_2': tbl_2, 'tbl_3': tbl_3, 'tbl_4': tbl_4, 'tbl_5': tbl_5, 'tbl_6': tbl_6, 'tbl_7': tbl_7, 'tbl_8': tbl_8, 'tbl_9': tbl_9, 'tbl_10': tbl_10, 'tbl_11': tbl_11, 'tbl_12': tbl_12, 'tbl_13': tbl_13, 'tbl_14': tbl_14, 'tbl_15': tbl_15, 'tbl_16': tbl_16, 'tbl_17': tbl_17, 'tbl_18': tbl_18, 'tbl_19': tbl_19, 'tbl_20': tbl_20, 'tbl_21': tbl_21, 'tbl_22': tbl_22, 'tbl_23': tbl_23, 'tbl_24': tbl_24, 'tbl_25': tbl_25, 'tbl_26': tbl_26, 'W_top1': W_top1, 'b_top1': b_top1, 'W_top2': W_top2, 'b_top2': b_top2, 'W_top3': W_top3}

def reference(dense_ctx, ids, tbl_0, tbl_1, tbl_2, tbl_3, tbl_4, tbl_5, tbl_6, tbl_7, tbl_8, tbl_9, tbl_10, tbl_11, tbl_12, tbl_13, tbl_14, tbl_15, tbl_16, tbl_17, tbl_18, tbl_19, tbl_20, tbl_21, tbl_22, tbl_23, tbl_24, tbl_25, tbl_26, W_top1, b_top1, W_top2, b_top2, W_top3):
    import jax
    import jax.numpy as jnp

    def _L0_rec_ref(inputs):
        import jax, jax.numpy as jnp
        import numpy as np
        NUM_FEATURES = 27
        EMBED_DIM = 128
        BATCH = 4096
        interactions = jnp.einsum('bnd,bmd->bnm', inputs, inputs)
        n = inputs.shape[1]
        i, j = jnp.triu_indices(n, k=1)
        return interactions[:, i, j]
    e = jnp.stack([tbl_0[ids[:, 0]], tbl_1[ids[:, 1]], tbl_2[ids[:, 2]], tbl_3[ids[:, 3]], tbl_4[ids[:, 4]], tbl_5[ids[:, 5]], tbl_6[ids[:, 6]], tbl_7[ids[:, 7]], tbl_8[ids[:, 8]], tbl_9[ids[:, 9]], tbl_10[ids[:, 10]], tbl_11[ids[:, 11]], tbl_12[ids[:, 12]], tbl_13[ids[:, 13]], tbl_14[ids[:, 14]], tbl_15[ids[:, 15]], tbl_16[ids[:, 16]], tbl_17[ids[:, 17]], tbl_18[ids[:, 18]], tbl_19[ids[:, 19]], tbl_20[ids[:, 20]], tbl_21[ids[:, 21]], tbl_22[ids[:, 22]], tbl_23[ids[:, 23]], tbl_24[ids[:, 24]], tbl_25[ids[:, 25]], tbl_26[ids[:, 26]]], axis=1)
    z = _L0_rec_ref(e)
    z = z.reshape(z.shape[0], -1)
    h = jnp.concatenate([z, dense_ctx], axis=1)
    h = jnp.maximum(h @ W_top1 + b_top1, 0.0)
    h = jnp.maximum(h @ W_top2 + b_top2, 0.0)
    y = h @ W_top3
    return y

_drawn_inputs = setup_inputs


def setup_inputs(seed=0):
    import zlib

    import numpy as np

    out = dict(_drawn_inputs(seed))
    spreads = {'b_top1': (0.0, 0.1), 'b_top2': (0.0, 0.1)}
    factors = {}
    for name, (base, spread) in spreads.items():
        noise = np.random.default_rng([zlib.crc32(name.encode()), seed]).standard_normal(out[name].shape)
        drawn = base * np.exp(spread * noise) if base else spread * noise
        out[name] = jnp.asarray(drawn.astype(out[name].dtype))
    for name, factor in factors.items():
        out[name] = (out[name] * factor).astype(out[name].dtype)
    return out
```

```python
from contextlib import ExitStack

import numpy as np

import concourse.bass as bass
from concourse import mybir
from concourse.alu_op_type import AluOpType as ALU

ACT = mybir.ActivationFunctionType
F32 = mybir.dt.float32
F32R = mybir.dt.float32r
I32 = mybir.dt.int32

P = 128
Q = 32
BATCH = 2048
FEATS = 27
DENSE = 16
HID1 = 512
HID2 = 256
PAIR = 2 * P
TURNS = BATCH // PAIR

BANK = 512
PER_BANK = BANK // P
GROUPS = [(f, min(PER_BANK, FEATS - f)) for f in range(0, FEATS, PER_BANK)]
NG = len(GROUPS)

COLS = FEATS - 1
QUADS = P // Q
BLOCK = QUADS * COLS
GRAMS_BANK = BANK // BLOCK
FILL_BANKS = 2
GRAMS_FILL = FILL_BANKS * GRAMS_BANK
FILL_SAMPLES = GRAMS_FILL * QUADS
FILLS = P // FILL_SAMPLES

SLOTS = -(-COLS // QUADS)
DENSE_SLOT = COLS - SLOTS * (QUADS - 1)
SLOT_COLS = [min(SLOTS, COLS - SLOTS * g) for g in range(QUADS)]
assert DENSE_SLOT == SLOTS - 2

K1 = HID1 // P
K2 = HID2 // P
JOB = BANK // PAIR
assert K1 == 2 * JOB and K2 == JOB


def lay_w1(w):
    rows = np.zeros((P, SLOTS, HID1), w.dtype)
    row_of = {(n, m): r for r, (n, m) in enumerate(zip(*np.triu_indices(FEATS, k=1)))}
    for g in range(QUADS):
        for j in range(SLOT_COLS[g]):
            m = 1 + SLOTS * g + j
            for n in range(m):
                rows[Q * g + n, j] = w[row_of[n, m]]
    first = Q * (QUADS - 1)
    rows[first : first + DENSE, DENSE_SLOT] = w[len(row_of) :]
    return rows


def build(nc, ids, dense_t, tables, w1, b1, w2, b2, w3, y):
    with ExitStack() as ctx:

        def sb(name, shape, dt=F32):
            return ctx.enter_context(nc.sbuf_tensor(name, shape, dt))

        def ps(name, shape):
            return ctx.enter_context(nc.psum_tensor(name, shape, F32))

        def sem(name):
            return ctx.enter_context(nc.semaphore(name))

        idt = [sb(f"idt{h}", [P, FEATS], I32) for h in range(2)]
        rows = [sb(f"rows{h}", [P, FEATS * P]) for h in range(2)]
        ident = sb("ident", [P, P])
        emb_hi = sb("emb_hi", [P, P, Q], F32R)
        emb_lo = sb("emb_lo", [P, P, Q], F32R)
        z = sb("z", [P, SLOTS, PAIR])
        z_hi = sb("z_hi", [P, SLOTS, PAIR], F32R)
        z_lo = sb("z_lo", [P, SLOTS, PAIR], F32R)
        w1_raw = sb("w1_raw", [P, SLOTS, HID1])
        w1_hi = sb("w1_hi", [P, SLOTS, HID1], F32R)
        w1_lo = sb("w1_lo", [P, SLOTS, HID1], F32R)
        w2_sb = sb("w2_sb", [P, K1, HID2])
        w3_sb = sb("w3_sb", [P, K2])
        b1_sb = sb("b1_sb", [P, K1])
        b2_sb = sb("b2_sb", [P, K2])
        h1 = sb("h1", [P, K1, PAIR])
        h2 = sb("h2", [P, K2, PAIR])
        y_sb = sb("y_sb", [1, BATCH])

        turned = [ps(f"turned{k}", [P, BANK]) for k in range(2)]
        gram = [ps(f"gram{k}", [P, FILL_BANKS, BANK]) for k in range(2)]
        mlp_ps = [ps(f"mlp_ps{k}", [P, JOB, PAIR]) for k in range(2)]

        ids_in = [sem(f"ids_in{h}") for h in range(2)]
        rows_in = [[sem(f"rows_in{h}_{k}") for k in range(NG)] for h in range(2)]
        dense_in = sem("dense_in")
        w_in = sem("w_in")
        pool_marks = sem("pool_marks")
        sp_marks = sem("sp_marks")
        small_in = sem("small_in")
        zeroed = sem("zeroed")
        ident_made = sem("ident_made")
        w1_hi_made = sem("w1_hi_made")
        w1_lo_made = sem("w1_lo_made")
        turned_full = sem("turned_full")
        hi_out = sem("hi_out")
        lo_out = sem("lo_out")
        gram_full = sem("gram_full")
        z_act = sem("z_act")
        z_dve = sem("z_dve")
        z_hi_made = sem("z_hi_made")
        z_lo_made = sem("z_lo_made")
        h1_full = sem("h1_full")
        h1_act = sem("h1_act")
        h1_dve = sem("h1_dve")
        h2_full = sem("h2_full")
        h2_out = sem("h2_out")
        y_full = sem("y_full")
        y_out = sem("y_out")
        y_stored = sem("y_stored")

        def lookups(i, h):
            return 2 * i + h

        def peeled(engine, turn):
            turn(0, True)
            with engine.Fori(1, TURNS) as i:
                turn(i, False)

        block = ctx.enter_context(nc.Block())

        @block.sync
        def _(sp):
            def load_ids(i, h, first):
                at = lookups(i, h) * P if first else sp.snap(lookups(i, h) * P)
                if not first:
                    sp.wait_ge(turned_full, sp.snap(NG * (lookups(i, h) - 1)))
                    sp.sem_inc(sp_marks, 1)
                sp.dma_start(idt[h][:, :], ids[bass.ds(at, P), :]).then_inc(ids_in[h], 16)

            load_ids(0, 0, True)
            load_ids(0, 1, True)
            sp.dma_start(w1_raw[:, :, :], w1).then_inc(w_in, 16)
            sp.dma_start(w2_sb[:, :, :], w2.rearrange("(k p) n -> p k n", p=P)).then_inc(small_in, 16)
            sp.dma_start(w3_sb[:, :], w3).then_inc(small_in, 16)
            sp.dma_start(b1_sb[:, :], b1).then_inc(small_in, 16)
            sp.dma_start(b2_sb[:, :], b2).then_inc(small_in, 16)

            dense_at = Q * (QUADS - 1)

            def load_dense(i, first):
                at = i * PAIR if first else sp.snap(i * PAIR)
                if first:
                    sp.wait_ge(zeroed, 3)
                else:
                    sp.wait_ge(z_lo_made, sp.snap(2 * i))
                    sp.sem_inc(sp_marks, 1)
                sp.dma_start(
                    z[dense_at : dense_at + DENSE, DENSE_SLOT, :], dense_t[:, bass.ds(at, PAIR)]
                ).then_inc(dense_in, 16)

            load_dense(0, True)
            with sp.Fori(1, TURNS) as i:
                load_ids(i, 0, False)
                load_ids(i, 1, False)
                load_dense(i, False)
            sp.wait_ge(y_out, TURNS)
            sp.dma_start(y, y_sb[:, :]).then_inc(y_stored, 16)
            sp.wait_ge(y_stored, 16)

        @block.gpsimd
        def _(pool):
            def gather(i, h, first):
                pool.wait_ge(ids_in[h], 16 * (i + 1))
                if not first:
                    pool.wait_ge(turned_full, NG * (lookups(i, h) - 1))
                pool.sem_inc(pool_marks, 1)
                for k, (f0, n) in enumerate(GROUPS):
                    for f in range(f0, f0 + n):
                        pool.indirect_dma_start(
                            rows[h][:, f * P : (f + 1) * P],
                            None,
                            tables[f],
                            bass.IndirectOffsetOnAxis(ap=idt[h][:, f : f + 1], axis=0),
                        ).then_inc(rows_in[h][k], 16)

            pool.memset(emb_hi[:, :, FEATS:Q].bitcast(F32), 0.0).then_inc(zeroed, 1)
            pool.memset(emb_lo[:, :, FEATS:Q].bitcast(F32), 0.0).then_inc(zeroed, 1)
            pool.wait_ge(zeroed, 2)
            pool.memset(z[Q * (QUADS - 1) : P, DENSE_SLOT:SLOTS, :], 0.0).then_inc(zeroed, 1)
            pool.wait_ge(zeroed, 3)
            pool.memset(ident[:, :], 0.0).then_inc(ident_made, 1)
            pool.wait_ge(ident_made, 1)
            pool.affine_select(
                out=ident[:, :], in_=ident[:, :], compare_op=ALU.not_equal, fill=1.0,
                base=0, pattern=[[-1, P]], channel_multiplier=1,
            ).then_inc(ident_made, 1)

            def turn(i, first):
                gather(i, 0, first)
                gather(i, 1, first)

            peeled(pool, turn)

        def take_fill(engine, copy, i, h, q):
            n = FILLS * lookups(i, h) + q
            engine.wait_ge(gram_full, n + 1)
            full = gram[q % 2][:, :, 0 : GRAMS_BANK * BLOCK].rearrange("p k (g s m) -> p k g s m", s=QUADS, m=COLS)
            at = h * P + q * FILL_SAMPLES
            to = z[:, :, at : at + FILL_SAMPLES].rearrange("p j (k g s) -> p k g s j", k=FILL_BANKS, s=QUADS)
            for s in range(QUADS):
                for g in range(QUADS):
                    m0, n_m = SLOTS * g, SLOT_COLS[g]
                    last = copy(
                        to[Q * g : Q * (g + 1), :, :, s, 0:n_m],
                        full[Q * s : Q * (s + 1), :, :, s, m0 : m0 + n_m],
                    )
            return last

        @block.scalar
        def _(act):
            def copy(out, in_):
                return act.activation(out, in_, ACT.Copy)

            def upper_parts(i, h, first):
                if not (first and h == 0):
                    act.wait_ge(gram_full, FILLS * lookups(i, h))
                for k, (f0, n) in enumerate(GROUPS):
                    act.wait_ge(turned_full, NG * lookups(i, h) + k + 1)
                    act.activation(
                        emb_hi[:, :, f0 : f0 + n],
                        turned[(NG * h + k) % 2][:, 0 : n * P].rearrange("p (f b) -> p b f", b=P),
                        ACT.Copy,
                    ).then_inc(hi_out, 1)

            def z_parts(i, h, first):
                if not first:
                    act.wait_ge(z_lo_made, 2 * i)
                for q in range(0, FILLS, 2):
                    take_fill(act, copy, i, h, q).then_inc(z_act, 1)
                act.wait_ge(z_act, FILLS // 2 * (lookups(i, h) + 1))
                act.wait_ge(z_dve, FILLS // 2 * (lookups(i, h) + 1))
                if h == 0:
                    act.wait_ge(dense_in, 16 * (i + 1))
                act.activation(z_hi[:, :, h * P : (h + 1) * P], z[:, :, h * P : (h + 1) * P], ACT.Copy).then_inc(
                    z_hi_made, 1
                )

            def layer1(p):
                act.wait_ge(h1_full, 2 * p + 1)
                for c in range(JOB):
                    last = act.activation(h1[:, c, :], mlp_ps[0][:, c, :], ACT.Relu, bias=b1_sb[:, c : c + 1])
                last.then_inc(h1_act, 1)

            def layer2(p):
                act.wait_ge(h2_full, p + 1)
                for c in range(K2):
                    last = act.activation(h2[:, c, :], mlp_ps[0][:, c, :], ACT.Relu, bias=b2_sb[:, c : c + 1])
                last.then_inc(h2_out, 1)

            def layer3(p):
                act.wait_ge(y_full, p + 1)
                act.activation(y_sb[:, bass.ds(p * PAIR, PAIR)], mlp_ps[1][0:1, 0, :], ACT.Copy).then_inc(y_out, 1)

            act.wait_ge(small_in, 64)
            act.wait_ge(zeroed, 3)
            act.wait_ge(w_in, 16)
            act.activation(w1_hi[:, :, :], w1_raw[:, :, :], ACT.Copy).then_inc(w1_hi_made, 1)

            def turn(i, first):
                upper_parts(i, 0, first)
                if not first:
                    layer1(i - 1)
                z_parts(i, 0, first)
                upper_parts(i, 1, first)
                if not first:
                    layer2(i - 1)
                z_parts(i, 1, first)
                if not first:
                    layer3(i - 1)

            peeled(act, turn)
            layer1(TURNS - 1)
            layer2(TURNS - 1)
            layer3(TURNS - 1)

        @block.vector
        def _(dve):
            def copy(out, in_):
                return dve.tensor_copy(out, in_)

            def lower_parts(i, h):
                for k, (f0, n) in enumerate(GROUPS):
                    dve.wait_ge(hi_out, NG * lookups(i, h) + k + 1)
                    dve.tensor_tensor(
                        emb_lo[:, :, f0 : f0 + n],
                        turned[(NG * h + k) % 2][:, 0 : n * P].rearrange("p (f b) -> p b f", b=P),
                        emb_hi[:, :, f0 : f0 + n].bitcast(F32),
                        ALU.subtract,
                    ).then_inc(lo_out, 1)

            def z_parts(i, h, first):
                if not first:
                    dve.wait_ge(z_lo_made, 2 * i)
                for q in range(1, FILLS, 2):
                    take_fill(dve, copy, i, h, q).then_inc(z_dve, 1)
                dve.wait_ge(z_hi_made, lookups(i, h) + 1)
                tile = slice(h * P, (h + 1) * P)
                dve.tensor_tensor(
                    z_lo[:, :, tile], z[:, :, tile], z_hi[:, :, tile].bitcast(F32), ALU.subtract
                ).then_inc(z_lo_made, 1)

            def layer1(p):
                dve.wait_ge(h1_full, 2 * p + 2)
                for c in range(JOB):
                    last = dve.tensor_scalar(
                        h1[:, JOB + c, :], mlp_ps[1][:, c, :], b1_sb[:, JOB + c : JOB + c + 1], 0.0, ALU.add, ALU.max
                    )
                last.then_inc(h1_dve, 1)

            dve.wait_ge(small_in, 64)
            dve.wait_ge(zeroed, 3)
            dve.wait_ge(w1_hi_made, 1)
            dve.tensor_tensor(w1_lo[:, :, :], w1_raw[:, :, :], w1_hi[:, :, :].bitcast(F32), ALU.subtract).then_inc(
                w1_lo_made, 1
            )

            def turn(i, first):
                lower_parts(i, 0)
                if not first:
                    layer1(i - 1)
                z_parts(i, 0, first)
                lower_parts(i, 1)
                z_parts(i, 1, first)

            peeled(dve, turn)
            layer1(TURNS - 1)

        @block.tensor
        def _(pe):
            def transposes(i, h, first):
                for k, (f0, n) in enumerate(GROUPS):
                    pe.wait_ge(rows_in[h][k], 16 * n * (i + 1))
                    if not (first and h == 0 and k < 2):
                        pe.wait_ge(lo_out, NG * lookups(i, h) + k - 1)
                    for c in range(n):
                        last = pe.transpose(
                            turned[(NG * h + k) % 2][:, c * P : (c + 1) * P],
                            rows[h][:, (f0 + c) * P : (f0 + c + 1) * P],
                            ident[:, :],
                        )
                    last.then_inc(turned_full, 1)

            def products(i, h, first):
                pe.wait_ge(lo_out, NG * (lookups(i, h) + 1))
                for q in range(FILLS):
                    if not (first and h == 0 and q < 2):
                        free = FILLS // 2 * lookups(i, h) + q // 2
                        pe.wait_ge(z_act if q % 2 == 0 else z_dve, free)
                    for n in range(GRAMS_FILL):
                        b0 = q * FILL_SAMPLES + n * QUADS
                        at = n % GRAMS_BANK * BLOCK
                        out = gram[q % 2][:, n // GRAMS_BANK, at : at + BLOCK]
                        for left, right in ((emb_hi, emb_hi), (emb_lo, emb_hi), (emb_hi, emb_lo)):
                            last = pe.matmul(
                                out,
                                left[:, b0 : b0 + QUADS, :],
                                right[:, b0 : b0 + QUADS, 1:FEATS],
                                start=left is emb_hi and right is emb_hi,
                                stop=right is emb_lo,
                            )
                    last.then_inc(gram_full, 1)

            def layer1(p, first):
                pe.wait_ge(z_lo_made, 2 * (p + 1))
                for half in range(2):
                    if not first:
                        pe.wait_ge(h2_out if half == 0 else y_out, p)
                    for c in range(JOB):
                        cols = slice((half * JOB + c) * P, (half * JOB + c + 1) * P)
                        for j in range(SLOTS):
                            used = P if j <= DENSE_SLOT else Q * (QUADS - 1)
                            for left, right in ((w1_hi, z_hi), (w1_lo, z_hi), (w1_hi, z_lo)):
                                last = pe.matmul(
                                    mlp_ps[half][:, c, :],
                                    left[0:used, j, cols],
                                    right[0:used, j, :],
                                    start=j == 0 and left is w1_hi and right is z_hi,
                                    stop=j == SLOTS - 1 and right is z_lo,
                                )
                    last.then_inc(h1_full, 1)

            def layer2(p):
                pe.wait_ge(h1_act, p + 1)
                pe.wait_ge(h1_dve, p + 1)
                for c in range(K2):
                    for k in range(K1):
                        last = pe.matmul(
                            mlp_ps[0][:, c, :], w2_sb[:, k, c * P : (c + 1) * P], h1[:, k, :],
                            start=k == 0, stop=k == K1 - 1,
                        )
                last.then_inc(h2_full, 1)

            def layer3(p):
                pe.wait_ge(h2_out, p + 1)
                for k in range(K2):
                    last = pe.matmul(
                        mlp_ps[1][0:1, 0, :], w3_sb[:, k : k + 1], h2[:, k, :], start=k == 0, stop=k == K2 - 1
                    )
                last.then_inc(y_full, 1)

            pe.wait_ge(ident_made, 2)
            pe.wait_ge(small_in, 64)
            pe.wait_ge(zeroed, 3)

            def turn(i, first, second=False):
                transposes(i, 0, first)
                if not first:
                    layer1(i - 1, second)
                products(i, 0, first)
                transposes(i, 1, first)
                if not first:
                    layer2(i - 1)
                products(i, 1, first)
                if not first:
                    layer3(i - 1)

            turn(0, True)
            pe.wait_ge(w1_lo_made, 1)
            turn(1, False, second=True)
            with pe.Fori(2, TURNS) as i:
                turn(i, False)
            layer1(TURNS - 1, False)
            layer2(TURNS - 1)
            layer3(TURNS - 1)


def kernel(**inputs):
    import numpy as _np
    import concourse.bacc as _bacc
    from concourse import mybir as _mybir
    from concourse.bass_utils import run_bass_kernel_spmd as _run

    nc = _bacc.Bacc("TRN2", target_bir_lowering=False, num_devices=1)
    arrays = {}

    def put(name, a):
        a = _np.ascontiguousarray(a)
        arrays[name] = a
        return nc.dram_tensor(name, a.shape, _mybir.dt.from_np(a.dtype), kind="ExternalInput").ap()

    get = lambda name: _np.asarray(inputs[name])
    y = nc.dram_tensor("y", (1, BATCH), F32, kind="ExternalOutput").ap()
    build(
        nc,
        ids=put("ids", get("ids")),
        dense_t=put("dense_t", get("dense_ctx").T),
        tables=[put(f"tbl_{f}", get(f"tbl_{f}")) for f in range(FEATS)],
        w1=put("w1", lay_w1(get("W_top1"))),
        b1=put("b1", get("b_top1").reshape(K1, P).T),
        w2=put("w2", get("W_top2")),
        b2=put("b2", get("b_top2").reshape(K2, P).T),
        w3=put("w3", get("W_top3").reshape(K2, P).T),
        y=y,
    )
    r = _run(nc, [arrays], core_ids=[0])
    return r.results[0]["y"].reshape(BATCH, 1)
```

```python
from contextlib import ExitStack

import numpy as np

import concourse.bass as bass
from concourse import mybir
from concourse.alu_op_type import AluOpType as ALU

ACT = mybir.ActivationFunctionType
F32 = mybir.dt.float32
F32R = mybir.dt.float32r
I32 = mybir.dt.int32

P = 128
Q = 32
BATCH = 2048
FEATS = 27
DENSE = 16
HID1 = 512
HID2 = 256
PAIR = 2 * P
TURNS = BATCH // PAIR
TILES = BATCH // P

ONEHOT = 6
GATHERED = FEATS - ONEHOT
SMALL = 1000
CHUNKS = 8
ROWS = SMALL // CHUNKS
assert ROWS * CHUNKS == SMALL and ROWS <= P
MASKS = 3
assert ONEHOT == 2 * MASKS
SPREADS = 2

BANK = 512
PER_BANK = BANK // P
NG = -(-GATHERED // PER_BANK)
GROUPS = [(GATHERED * k // NG, GATHERED * (k + 1) // NG - GATHERED * k // NG) for k in range(NG)]
assert NG == 6 and max(n for _, n in GROUPS) <= PER_BANK

JOBS = [("T", 0, 0), ("T", 0, 1), ("T", 0, 2), ("O", 0), ("O", 1), ("T", 0, 3), ("O", 2), ("T", 0, 4), ("O", 3)]
JOBS += [("O", 4), ("T", 0, 5), ("O", 5)] + [("T", 1, k) for k in range(NG)]
NJ = len(JOBS)
assert NJ % 2 == 0

COLS = FEATS - 1
QUADS = P // Q
BLOCK = QUADS * COLS
GRAMS_BANK = BANK // BLOCK
FILL_BANKS = 2
GRAMS_FILL = FILL_BANKS * GRAMS_BANK
FILL_SAMPLES = GRAMS_FILL * QUADS
FILLS = P // FILL_SAMPLES

SLOTS = -(-COLS // QUADS)
DENSE_SLOT = COLS - SLOTS * (QUADS - 1)
SLOT_COLS = [min(SLOTS, COLS - SLOTS * g) for g in range(QUADS)]
DENSE_AT = Q * (QUADS - 1)
assert DENSE_SLOT == SLOTS - 2

K1 = HID1 // P
K2 = HID2 // P
JOB = BANK // PAIR
assert K1 == 2 * JOB and K2 == JOB

PIECE = CHUNKS * P
RAWS = 2
W1_SLOTS = PIECE // HID1
W1_PIECES = [(j, min(W1_SLOTS, SLOTS - j)) for j in range(0, SLOTS, W1_SLOTS)]
assert K1 * HID2 == PIECE


def lay_w1(w):
    rows = np.zeros((P, SLOTS, HID1), w.dtype)
    row_of = {(n, m): r for r, (n, m) in enumerate(zip(*np.triu_indices(FEATS, k=1)))}
    for g in range(QUADS):
        for j in range(SLOT_COLS[g]):
            m = 1 + SLOTS * g + j
            for n in range(m):
                rows[Q * g + n, j] = w[row_of[n, m]]
    rows[DENSE_AT : DENSE_AT + DENSE, DENSE_SLOT] = w[len(row_of) :]
    return rows


def build(nc, ids, small_ids, dense_t, tables, w1, b1, w2, b2, w3, y):
    with ExitStack() as ctx:

        def sb(name, shape, dt=F32):
            return ctx.enter_context(nc.sbuf_tensor(name, shape, dt))

        def ps(name, shape):
            return ctx.enter_context(nc.psum_tensor(name, shape, F32))

        def sem(name):
            return ctx.enter_context(nc.semaphore(name))

        idt = [sb(f"idt{h}", [P, FEATS], I32) for h in range(2)]
        rows = [sb(f"rows{h}", [P, GATHERED * P]) for h in range(2)]
        ident = sb("ident", [P, P])
        raw = [sb(f"raw{k}", [P, PIECE]) for k in range(RAWS)]
        table_hi = sb("table_hi", [P, ONEHOT, CHUNKS, P], F32R)
        table_lo = sb("table_lo", [P, ONEHOT, CHUNKS, P], F32R)
        small_i = rows[1][0:ONEHOT, 0:BATCH].bitcast(I32)
        small_f = sb("small_f", [ONEHOT, BATCH], F32R)
        pick = sb("pick", [ONEHOT, ONEHOT, P], F32R)
        row_i = sb("row_i", [P, CHUNKS], I32)
        row_f = sb("row_f", [P, CHUNKS])
        mask = sb("mask", [P, MASKS, CHUNKS, PAIR], F32R)
        emb = sb("emb", [P, PAIR, Q])
        z = sb("z", [P, SLOTS, P])
        z_hi = sb("z_hi", [P, SLOTS, PAIR], F32R)
        z_lo = sb("z_lo", [P, SLOTS, PAIR], F32R)
        w1_hi = sb("w1_hi", [P, SLOTS, HID1], F32R)
        w1_lo = sb("w1_lo", [P, SLOTS, HID1], F32R)
        w2_hi = sb("w2_hi", [P, K1, HID2], F32R)
        w2_lo = sb("w2_lo", [P, K1, HID2], F32R)
        w3_sb = sb("w3_sb", [P, K2])
        b1_sb = sb("b1_sb", [P, K1])
        b2_sb = sb("b2_sb", [P, K2])
        h1_hi = sb("h1_hi", [P, K1, PAIR], F32R)
        h1_lo = sb("h1_lo", [P, K1, PAIR], F32R)
        h1 = raw[0][:, 0 : K1 * PAIR].rearrange("p (c b) -> p c b", c=K1)
        h2 = raw[1][:, 0 : K2 * PAIR].rearrange("p (c b) -> p c b", c=K2)
        pick_raw = z[0:ONEHOT, 0:ONEHOT, :]
        y_cols = sb("y_cols", [P, TILES])
        y_rows = sb("y_rows", [TILES, P])

        turned = [ps(f"turned{k}", [P, BANK]) for k in range(2)]
        gram = [ps(f"gram{k}", [P, FILL_BANKS, BANK]) for k in range(2)]
        mlp = ps("mlp", [P, JOB, PAIR])
        spread = ps("spread", [P, SPREADS, PAIR])

        ids_in = [sem(f"ids_in{h}") for h in range(2)]
        rows_in = [[sem(f"rows_in{h}_{k}") for k in range(NG)] for h in range(2)]
        raw_in = [sem(f"raw_in{k}") for k in range(RAWS)]
        hi_cut = sem("hi_cut")
        lo_cut = sem("lo_cut")
        dense_in = sem("dense_in")
        small_ids_in = sem("small_ids_in")
        small_ids_cast = sem("small_ids_cast")
        small_in = sem("small_in")
        emb_zeroed = sem("emb_zeroed")
        z_zeroed = sem("z_zeroed")
        ident_made = sem("ident_made")
        pick_made = sem("pick_made")
        row_made = sem("row_made")
        consts_made = sem("consts_made")
        spread_full = sem("spread_full")
        mask_made = sem("mask_made")
        turned_full = sem("turned_full")
        turned_out = sem("turned_out")
        gram_full = sem("gram_full")
        z_act = sem("z_act")
        z_dve = sem("z_dve")
        z_hi_made = sem("z_hi_made")
        z_lo_made = sem("z_lo_made")
        h1_full = sem("h1_full")
        h1_hi_made = sem("h1_hi_made")
        h1_read = sem("h1_read")
        h1_lo_made = sem("h1_lo_made")
        h2_full = sem("h2_full")
        h2_out = sem("h2_out")
        y_full = sem("y_full")
        y_out = sem("y_out")
        y_turned = sem("y_turned")
        y_rows_made = sem("y_rows_made")
        y_stored = sem("y_stored")
        pool_marks = sem("pool_marks")
        sp_marks = sem("sp_marks")
        pe_marks = sem("pe_marks")

        def tile_of(i, h):
            return 2 * i + h

        def turned_by(i, job):
            return NJ * i + JOBS.index(job) + 1

        table_pieces = [
            (
                lambda r, k=k: r[0:ROWS, :].rearrange("p (c d) -> p c d", c=CHUNKS),
                tables[GATHERED + k].rearrange("(p c) d -> p c d", c=CHUNKS),
                table_hi[0:ROWS, k],
                table_lo[0:ROWS, k],
            )
            for k in range(ONEHOT)
        ]
        w1_pieces = [
            (
                lambda r, n=n: r[:, 0 : n * HID1].rearrange("p (j o) -> p j o", j=n),
                w1[:, j : j + n],
                w1_hi[:, j : j + n],
                w1_lo[:, j : j + n],
            )
            for j, n in W1_PIECES
        ]
        w2_pieces = [
            (
                lambda r: r[:, :].rearrange("p (k n) -> p k n", k=K1),
                w2.rearrange("(k p) n -> p k n", p=P),
                w2_hi[:, :, :],
                w2_lo[:, :, :],
            )
        ]
        pieces = table_pieces + w1_pieces + w2_pieces

        def some(first, count):
            return list(enumerate(pieces))[first : first + count]

        block = ctx.enter_context(nc.Block())

        @block.sync
        def _(sp):
            def load_ids(i, h, first):
                at = tile_of(i, h) * P if first else sp.snap(tile_of(i, h) * P)
                if not first:
                    for k, (_, n) in enumerate(GROUPS):
                        sp.wait_ge(rows_in[h][k], sp.snap(16 * n * i))
                        sp.sem_inc(sp_marks, 1)
                sp.dma_start(idt[h][:, :], ids[bass.ds(at, P), :]).then_inc(ids_in[h], 16)

            def load_dense(i, h, first):
                at = tile_of(i, h) * P if first else sp.snap(tile_of(i, h) * P)
                if first and h == 0:
                    sp.wait_ge(z_zeroed, 1)
                else:
                    sp.wait_ge(z_lo_made, tile_of(i, h) if first else sp.snap(tile_of(i, h)))
                    sp.sem_inc(sp_marks, 1)
                sp.dma_start(
                    z[DENSE_AT : DENSE_AT + DENSE, DENSE_SLOT, :], dense_t[:, bass.ds(at, P)]
                ).then_inc(dense_in, 16)

            def load_pieces(which):
                for n, (as_loaded, source, _, _) in which:
                    if n >= RAWS:
                        sp.wait_ge(lo_cut, n - RAWS + 1)
                    sp.dma_start(as_loaded(raw[n % RAWS]), source).then_inc(raw_in[n % RAWS], 16)

            load_ids(0, 0, True)
            load_ids(0, 1, True)
            sp.dma_start(small_i, small_ids).then_inc(small_ids_in, 16)
            load_pieces(some(0, ONEHOT))
            load_dense(0, 0, True)
            sp.dma_start(w3_sb[:, :], w3).then_inc(small_in, 16)
            sp.dma_start(b1_sb[:, :], b1).then_inc(small_in, 16)
            sp.dma_start(b2_sb[:, :], b2).then_inc(small_in, 16)
            load_pieces(some(ONEHOT, len(pieces)))
            load_ids(1, 0, False)
            load_dense(0, 1, True)
            load_ids(1, 1, False)
            load_dense(1, 0, False)
            with sp.Fori(2, TURNS) as i:
                load_ids(i, 0, False)
                load_ids(i, 1, False)
                load_dense(i - 1, 1, False)
                load_dense(i, 0, False)
            load_dense(TURNS - 1, 1, False)
            sp.wait_ge(y_rows_made, 1)
            sp.dma_start(y, y_rows[:, :]).then_inc(y_stored, 16)
            sp.wait_ge(y_stored, 16)

        @block.gpsimd
        def _(pool):
            def gather(i, h, first):
                pool.wait_ge(ids_in[h], 16 * (i + 1))
                if first and h == 1:
                    pool.wait_ge(small_ids_cast, 1)
                for k, (f0, n) in enumerate(GROUPS):
                    if not first:
                        pool.wait_ge(turned_full, turned_by(i - 1, ("T", h, k)))
                        pool.sem_inc(pool_marks, 1)
                    for f in range(f0, f0 + n):
                        pool.indirect_dma_start(
                            rows[h][:, f * P : (f + 1) * P],
                            None,
                            tables[f],
                            bass.IndirectOffsetOnAxis(ap=idt[h][:, f : f + 1], axis=0),
                        ).then_inc(rows_in[h][k], 16)

            pool.memset(pick_raw, 0.0).then_inc(pick_made, 1)
            pool.iota(row_i[:, :], pattern=[[1, CHUNKS]], base=0, channel_multiplier=CHUNKS).then_inc(row_made, 1)
            pool.wait_ge(pick_made, 1)
            pool.affine_select(
                out=pick_raw, in_=pick_raw, compare_op=ALU.not_equal, fill=1.0,
                base=0, pattern=[[-1, ONEHOT], [0, P]], channel_multiplier=1,
            ).then_inc(pick_made, 1)
            pool.memset(ident[:, :], 0.0).then_inc(ident_made, 1)
            pool.wait_ge(ident_made, 1)
            pool.affine_select(
                out=ident[:, :], in_=ident[:, :], compare_op=ALU.not_equal, fill=1.0,
                base=0, pattern=[[-1, P]], channel_multiplier=1,
            ).then_inc(ident_made, 1)

            def turn(i, first):
                gather(i, 0, first)
                gather(i, 1, first)

            turn(0, True)
            with pool.Fori(1, TURNS) as i:
                turn(i, False)

        def take_fill(engine, copy, i, h, q):
            engine.wait_ge(gram_full, FILLS * tile_of(i, h) + q + 1)
            full = gram[q % 2][:, :, 0 : GRAMS_BANK * BLOCK].rearrange("p k (g s m) -> p k g s m", s=QUADS, m=COLS)
            to = z[:, :, q * FILL_SAMPLES : (q + 1) * FILL_SAMPLES]
            to = to.rearrange("p j (k g s) -> p k g s j", k=FILL_BANKS, s=QUADS)
            for s in range(QUADS):
                for g in range(QUADS):
                    m0, n_m = SLOTS * g, SLOT_COLS[g]
                    last = copy(
                        to[Q * g : Q * (g + 1), :, :, s, 0:n_m],
                        full[Q * s : Q * (s + 1), :, :, s, m0 : m0 + n_m],
                    )
            return last

        @block.scalar
        def _(act):
            def copy(out, in_):
                return act.activation(out, in_, ACT.Copy)

            def cut_hi(which):
                for n, (as_loaded, _, hi, _) in which:
                    act.wait_ge(raw_in[n % RAWS], 16 * (n // RAWS + 1))
                    copy(hi, as_loaded(raw[n % RAWS])).then_inc(hi_cut, 1)

            def to_emb(i, first, jobs):
                for job in jobs:
                    bank = turned[JOBS.index(job) % 2]
                    act.wait_ge(turned_full, turned_by(i, job))
                    if job[0] == "T":
                        _, h, k = job
                        f0, n = GROUPS[k]
                        if k == 0 and not first:
                            act.wait_ge(gram_full, FILLS * (tile_of(i, h) - 1))
                        out = emb[:, h * P : (h + 1) * P, f0 : f0 + n]
                        copy(out, bank[:, 0 : n * P].rearrange("p (f b) -> p b f", b=P)).then_inc(turned_out, 1)
                    else:
                        f = GATHERED + job[1]
                        if job[1] == 0 and not first:
                            act.wait_ge(gram_full, FILLS * tile_of(i, 0))
                        copy(emb[:, :, f], bank[:, 0:PAIR]).then_inc(turned_out, 1)

            def fill(i, h, q):
                if q == 0 and not (h == 0 and isinstance(i, int) and i == 0):
                    act.wait_ge(z_lo_made, tile_of(i, h))
                take_fill(act, copy, i, h, q).then_inc(z_act, 1)

            def cut_z_hi(i, h):
                act.wait_ge(z_act, FILLS // 2 * (tile_of(i, h) + 1))
                act.wait_ge(z_dve, FILLS // 2 * (tile_of(i, h) + 1))
                act.wait_ge(dense_in, 16 * (tile_of(i, h) + 1))
                copy(z_hi[:, :, h * P : (h + 1) * P], z[:, :, :]).then_inc(z_hi_made, 1)

            def layer1(p, half):
                act.wait_ge(h1_full, 2 * p + half + 1)
                for c in range(JOB):
                    k = half * JOB + c
                    last = act.activation(h1_hi[:, k, :], mlp[:, c, :], ACT.Relu, bias=b1_sb[:, k : k + 1])
                last.then_inc(h1_hi_made, 1)

            def layer2(p):
                act.wait_ge(h2_full, p + 1)
                for c in range(K2):
                    last = act.activation(h2[:, c, :], mlp[:, c, :], ACT.Relu, bias=b2_sb[:, c : c + 1])
                last.then_inc(h2_out, 1)

            def layer3(p):
                act.wait_ge(y_full, p + 1)
                copy(y_cols[:, bass.ds(2 * p, 2)], mlp[:, 0, 0:2]).then_inc(y_out, 1)

            def turn(i, first, second=False):
                to_emb(i, first, JOBS[0:1])
                if not first:
                    fill(i - 1, 1, 0)
                to_emb(i, first, JOBS[1:2])
                if not first:
                    fill(i - 1, 1, 2)
                    if not second:
                        layer3(i - 2)
                to_emb(i, first, JOBS[2:3])
                if not first:
                    cut_z_hi(i - 1, 1)
                to_emb(i, first, JOBS[3:12])
                if first:
                    cut_hi(some(ONEHOT, len(pieces)))
                if not first:
                    layer1(i - 1, 0)
                to_emb(i, first, JOBS[12:13])
                fill(i, 0, 0)
                to_emb(i, first, JOBS[13:14])
                fill(i, 0, 2)
                to_emb(i, first, JOBS[14:15])
                if not first:
                    layer1(i - 1, 1)
                to_emb(i, first, JOBS[15:17])
                cut_z_hi(i, 0)
                to_emb(i, first, JOBS[17:])
                if not first:
                    layer2(i - 1)

            cut_hi(some(0, ONEHOT))
            act.wait_ge(emb_zeroed, 1)
            act.wait_ge(z_zeroed, 1)
            turn(0, True)
            act.wait_ge(small_in, 48)
            act.wait_ge(lo_cut, len(pieces))
            turn(1, False, second=True)
            with act.Fori(2, TURNS) as i:
                turn(i, False)
            layer3(TURNS - 2)
            fill(TURNS - 1, 1, 0)
            fill(TURNS - 1, 1, 2)
            cut_z_hi(TURNS - 1, 1)
            layer1(TURNS - 1, 0)
            layer1(TURNS - 1, 1)
            layer2(TURNS - 1)
            layer3(TURNS - 1)
            act.wait_ge(y_turned, 1)
            copy(y_rows[:, :], mlp[0:TILES, 0, 0:P]).then_inc(y_rows_made, 1)

        @block.vector
        def _(dve):
            def copy(out, in_):
                return dve.tensor_copy(out, in_)

            def cut_lo(which):
                for n, (as_loaded, _, hi, lo) in which:
                    dve.wait_ge(hi_cut, n + 1)
                    dve.tensor_tensor(lo, as_loaded(raw[n % RAWS]), hi.bitcast(F32), ALU.subtract).then_inc(lo_cut, 1)

            def one_hot(i, k, used_in=None):
                if used_in is not None:
                    dve.wait_ge(turned_full, turned_by(used_in, ("O", (k - MASKS) % ONEHOT)))
                dve.wait_ge(spread_full, ONEHOT // SPREADS * i + k // SPREADS + 1)
                for c in range(CHUNKS):
                    last = dve.tensor_scalar(
                        mask[0:ROWS, k % MASKS, c, :], spread[0:ROWS, k % SPREADS, :], row_f[0:ROWS, c : c + 1], None,
                        ALU.is_equal,
                    )
                last.then_inc(mask_made, 1)

            def fill(i, h, q):
                if q == 1 and not (h == 0 and isinstance(i, int) and i == 0):
                    dve.wait_ge(z_lo_made, tile_of(i, h))
                take_fill(dve, copy, i, h, q).then_inc(z_dve, 1)

            def cut_z_lo(i, h):
                dve.wait_ge(z_hi_made, tile_of(i, h) + 1)
                tile = slice(h * P, (h + 1) * P)
                dve.tensor_tensor(z_lo[:, :, tile], z[:, :, :], z_hi[:, :, tile].bitcast(F32), ALU.subtract).then_inc(
                    z_lo_made, 1
                )

            def layer1(p, half):
                dve.wait_ge(h1_hi_made, 2 * p + half + 1)
                for c in range(JOB):
                    k = half * JOB + c
                    last = dve.tensor_scalar(h1[:, k, :], mlp[:, c, :], b1_sb[:, k : k + 1], 0.0, ALU.add, ALU.max)
                last.then_inc(h1_read, 1)
                dve.wait_ge(h1_read, 2 * p + half + 1)
                ks = slice(half * JOB, (half + 1) * JOB)
                dve.tensor_tensor(h1_lo[:, ks, :], h1[:, ks, :], h1_hi[:, ks, :].bitcast(F32), ALU.subtract).then_inc(
                    h1_lo_made, 1
                )

            def turn(i, first, last=False):
                if not first:
                    fill(i - 1, 1, 1)
                    fill(i - 1, 1, 3)
                one_hot(i, 3, used_in=i)
                if not first:
                    cut_z_lo(i - 1, 1)
                one_hot(i, 4, used_in=i)
                one_hot(i, 5, used_in=i)
                if first:
                    cut_lo(some(ONEHOT, len(pieces)))
                if not last:
                    one_hot(i + 1, 0, used_in=i)
                if not first:
                    layer1(i - 1, 0)
                fill(i, 0, 1)
                if not last:
                    one_hot(i + 1, 1, used_in=i)
                if not first:
                    layer1(i - 1, 1)
                fill(i, 0, 3)
                cut_z_lo(i, 0)
                if not last:
                    one_hot(i + 1, 2, used_in=i)

            dve.wait_ge(pick_made, 2)
            copy(pick[:, :, :], pick_raw).then_inc(consts_made, 1)
            dve.wait_ge(row_made, 1)
            copy(row_f[:, :], row_i[:, :]).then_inc(consts_made, 1)
            dve.memset(emb[:, :, FEATS:Q], 0.0).then_inc(emb_zeroed, 1)
            dve.memset(z[DENSE_AT:P, DENSE_SLOT:SLOTS, :], 0.0).then_inc(z_zeroed, 1)
            dve.wait_ge(small_ids_in, 16)
            copy(small_f[:, :], small_i).then_inc(small_ids_cast, 1)
            dve.wait_ge(consts_made, 2)
            for k in range(MASKS):
                one_hot(0, k)
            cut_lo(some(0, ONEHOT))
            turn(0, True)
            dve.wait_ge(small_in, 48)
            with dve.Fori(1, TURNS - 1) as i:
                turn(i, False)
            turn(TURNS - 1, False, last=True)
            fill(TURNS - 1, 1, 1)
            fill(TURNS - 1, 1, 3)
            cut_z_lo(TURNS - 1, 1)
            layer1(TURNS - 1, 0)
            layer1(TURNS - 1, 1)

        @block.tensor
        def _(pe):
            def transposes(i, h, k, first):
                f0, n = GROUPS[k]
                bank = turned_job(i, ("T", h, k), first)
                pe.wait_ge(rows_in[h][k], 16 * n * (i + 1))
                for c in range(n):
                    last = pe.transpose(
                        bank[:, c * P : (c + 1) * P], rows[h][:, (f0 + c) * P : (f0 + c + 1) * P], ident[:, :]
                    )
                last.then_inc(turned_full, 1)

            def turned_job(i, job, first):
                at = JOBS.index(job)
                if not (first and at < 2):
                    pe.wait_ge(turned_out, NJ * i + at - 1)
                return turned[at % 2]

            def lookup(i, k, first):
                bank = turned_job(i, ("O", k), first)
                if first:
                    pe.wait_ge(lo_cut, k + 1)
                pe.wait_ge(mask_made, ONEHOT * i + k + 1)
                for c in range(CHUNKS):
                    for part in (table_hi, table_lo):
                        last = pe.matmul(
                            bank[:, 0:PAIR], part[0:ROWS, k, c, :], mask[0:ROWS, k % MASKS, c, :],
                            start=c == 0 and part is table_hi, stop=c == CHUNKS - 1 and part is table_lo,
                        )
                last.then_inc(turned_full, 1)

            def spread_ids(i, k, first=False):
                if not first:
                    pe.wait_ge(mask_made, ONEHOT * i + k)
                    pe.sem_inc(pe_marks, 1)
                for n in range(SPREADS):
                    last = pe.matmul(
                        spread[:, n, :], pick[:, k + n, :], small_f[:, bass.ds(i * PAIR, PAIR)], start=True, stop=True
                    )
                last.then_inc(spread_full, 1)

            def fill(i, h, q):
                if q == 0:
                    pe.wait_ge(turned_out, turned_by(i, ("O", ONEHOT - 1) if h == 0 else ("T", 1, NG - 1)))
                if not (h == 0 and q < 2 and isinstance(i, int) and i == 0):
                    pe.wait_ge(z_act if q % 2 == 0 else z_dve, FILLS // 2 * tile_of(i, h) + q // 2)
                for n in range(GRAMS_FILL):
                    b0 = h * P + q * FILL_SAMPLES + n * QUADS
                    at = n % GRAMS_BANK * BLOCK
                    last = pe.matmul(
                        gram[q % 2][:, n // GRAMS_BANK, at : at + BLOCK],
                        emb[:, b0 : b0 + QUADS, :],
                        emb[:, b0 : b0 + QUADS, 1:FEATS],
                        start=True,
                        stop=True,
                    )
                last.then_inc(gram_full, 1)

            def layer1(p, c, first=False):
                half, place = divmod(c, JOB)
                if c == 0:
                    if not first:
                        pe.wait_ge(y_out, p)
                    pe.wait_ge(z_lo_made, 2 * (p + 1))
                elif place == 0:
                    pe.wait_ge(h1_read, 2 * p + 1)
                for j in range(SLOTS):
                    used = P if j <= DENSE_SLOT else DENSE_AT
                    for left, right in ((w1_hi, z_hi), (w1_lo, z_hi), (w1_hi, z_lo)):
                        last = pe.matmul(
                            mlp[:, place, :],
                            left[0:used, j, c * P : (c + 1) * P],
                            right[0:used, j, :],
                            start=j == 0 and left is w1_hi and right is z_hi,
                            stop=j == SLOTS - 1 and right is z_lo,
                        )
                if place == JOB - 1:
                    last.then_inc(h1_full, 1)

            def layer2(p):
                pe.wait_ge(h1_lo_made, 2 * (p + 1))
                for c in range(K2):
                    cols = slice(c * P, (c + 1) * P)
                    for k in range(K1):
                        for left, right in ((w2_hi, h1_hi), (w2_lo, h1_hi), (w2_hi, h1_lo)):
                            last = pe.matmul(
                                mlp[:, c, :],
                                left[:, k, cols],
                                right[:, k, :],
                                start=k == 0 and left is w2_hi and right is h1_hi,
                                stop=k == K1 - 1 and right is h1_lo,
                            )
                last.then_inc(h2_full, 1)

            def layer3(p):
                pe.wait_ge(h2_out, p + 1)
                for h in range(2):
                    for k in range(K2):
                        last = pe.matmul(
                            mlp[:, 0, h : h + 1], h2[:, k, h * P : (h + 1) * P], w3_sb[:, k : k + 1],
                            start=k == 0, stop=k == K2 - 1,
                        )
                last.then_inc(y_full, 1)

            def turn(i, first=False, second=False, last=False):
                transposes(i, 0, 0, first)
                if not first:
                    fill(i - 1, 1, 0)
                    fill(i - 1, 1, 1)
                transposes(i, 0, 1, first)
                if not first:
                    if not second:
                        layer3(i - 2)
                    fill(i - 1, 1, 2)
                    fill(i - 1, 1, 3)
                transposes(i, 0, 2, first)
                lookup(i, 0, first)
                lookup(i, 1, first)
                transposes(i, 0, 3, first)
                lookup(i, 2, first)
                spread_ids(i, 4)
                if second:
                    pe.wait_ge(lo_cut, len(pieces))
                    pe.wait_ge(small_in, 48)
                if not first:
                    layer1(i - 1, 0, second)
                transposes(i, 0, 4, first)
                lookup(i, 3, first)
                lookup(i, 4, first)
                transposes(i, 0, 5, first)
                lookup(i, 5, first)
                if not last:
                    spread_ids(i + 1, 0)
                if not first:
                    layer1(i - 1, 1)
                transposes(i, 1, 0, first)
                fill(i, 0, 0)
                fill(i, 0, 1)
                transposes(i, 1, 1, first)
                if not first:
                    layer1(i - 1, 2)
                fill(i, 0, 2)
                transposes(i, 1, 2, first)
                if not first:
                    layer1(i - 1, 3)
                if not last:
                    spread_ids(i + 1, 2)
                fill(i, 0, 3)
                for k in (3, 4, 5):
                    transposes(i, 1, k, first)
                if not first:
                    layer2(i - 1)

            pe.wait_ge(consts_made, 2)
            pe.wait_ge(small_ids_cast, 1)
            spread_ids(0, 0, first=True)
            spread_ids(0, 2)
            pe.wait_ge(ident_made, 2)
            pe.wait_ge(emb_zeroed, 1)
            turn(0, first=True)
            turn(1, second=True)
            with pe.Fori(2, TURNS - 1) as i:
                turn(i)
            turn(TURNS - 1, last=True)
            layer3(TURNS - 2)
            for q in range(FILLS):
                fill(TURNS - 1, 1, q)
            for c in range(K1):
                layer1(TURNS - 1, c)
            layer2(TURNS - 1)
            layer3(TURNS - 1)
            pe.wait_ge(y_out, TURNS)
            pe.transpose(mlp[0:TILES, 0, 0:P], y_cols[:, :], ident[:, :]).then_inc(y_turned, 1)


def kernel(**inputs):
    import numpy as _np
    import concourse.bacc as _bacc
    from concourse import mybir as _mybir
    from concourse.bass_utils import run_bass_kernel_spmd as _run

    nc = _bacc.Bacc("TRN2", target_bir_lowering=False, num_devices=1)
    arrays = {}

    def put(name, a):
        a = _np.ascontiguousarray(a)
        arrays[name] = a
        return nc.dram_tensor(name, a.shape, _mybir.dt.from_np(a.dtype), kind="ExternalInput").ap()

    get = lambda name: _np.asarray(inputs[name])
    y = nc.dram_tensor("y", (TILES, P), F32, kind="ExternalOutput").ap()
    build(
        nc,
        ids=put("ids", get("ids")),
        small_ids=put("small_ids", get("ids")[:, GATHERED:].T),
        dense_t=put("dense_t", get("dense_ctx").T),
        tables=[put(f"tbl_{f}", get(f"tbl_{f}")) for f in range(FEATS)],
        w1=put("w1", lay_w1(get("W_top1"))),
        b1=put("b1", get("b_top1").reshape(K1, P).T),
        w2=put("w2", get("W_top2")),
        b2=put("b2", get("b_top2").reshape(K2, P).T),
        w3=put("w3", get("W_top3").reshape(K2, P).T),
        y=y,
    )
    r = _run(nc, [arrays], core_ids=[0])
    return r.results[0]["y"].reshape(BATCH, 1)
```

```python
from contextlib import ExitStack

import numpy as np

import concourse.bass as bass
from concourse import mybir
from concourse.alu_op_type import AluOpType as ALU

ACT = mybir.ActivationFunctionType
F32 = mybir.dt.float32
F32R = mybir.dt.float32r
I32 = mybir.dt.int32

P = 128
Q = 32
BATCH = 2048
FEATS = 27
DENSE = 16
HID1 = 512
HID2 = 256
PAIR = 2 * P
TURNS = BATCH // PAIR
TILES = BATCH // P

ONEHOT = 7
GATHERED = FEATS - ONEHOT
SMALL = 1000
CHUNKS = 8
ROWS = SMALL // CHUNKS
assert ROWS * CHUNKS == SMALL and ROWS <= P
MASKS = 4
assert MASKS <= ONEHOT <= 2 * MASKS
BANK_TABLES = 2
LOOKUPS = [list(range(k, min(k + BANK_TABLES, ONEHOT))) for k in range(0, ONEHOT, BANK_TABLES)]

BANK = 512
PER_BANK = BANK // P
NG = -(-GATHERED // PER_BANK)
GROUPS = [(GATHERED * k // NG, GATHERED * (k + 1) // NG - GATHERED * k // NG) for k in range(NG)]
assert NG == 5 and max(n for _, n in GROUPS) <= PER_BANK

JOBS = [("T", 0, 0), ("T", 0, 1), ("T", 0, 2), ("O", 0), ("T", 0, 3), ("O", 1), ("T", 0, 4), ("O", 2), ("O", 3)]
JOBS += [("T", 1, k) for k in range(NG)]
NJ = len(JOBS)
assert NJ % 2 == 0

COLS = FEATS
QUADS = P // Q
BLOCK = QUADS * COLS
GRAMS_BANK = BANK // BLOCK
FILL_BANKS = 2
GRAMS_FILL = FILL_BANKS * GRAMS_BANK
FILL_SAMPLES = GRAMS_FILL * QUADS
FILLS = P // FILL_SAMPLES
assert FILLS == 4
LAST_SAMPLES = (FILLS - 1) * FILL_SAMPLES
ACT_FILLS = FILLS - 1

SLOTS = -(-COLS // QUADS)
SLOT_COLS = [min(SLOTS, COLS - SLOTS * g) for g in range(QUADS)]
DENSE_AT = Q * (QUADS - 1)
DENSE_SLOT = SLOTS - 1
assert SLOT_COLS[-1] == DENSE_SLOT and 2 * DENSE == Q

K1 = HID1 // P
K2 = HID2 // P
JOB = BANK // PAIR
assert K1 == 2 * JOB and K2 == JOB

PIECE = CHUNKS * P
RAWS = 2
PLACES = [0, 1, 2, 3]
assert 2 * HID1 == PIECE and K1 * HID2 == PIECE
PIECES = ONEHOT + SLOTS + 1
PLACES += [n % RAWS for n in range(PIECES - 1 - len(PLACES))]
PLACES += [1]


def lay_w1(w):
    rows = np.zeros((P, SLOTS, 2, HID1), w.dtype)
    row_of = {(n, m): r for r, (n, m) in enumerate(zip(*np.triu_indices(FEATS, k=1)))}
    for g in range(QUADS):
        for j in range(SLOT_COLS[g]):
            m = SLOTS * g + j
            for n in range(m):
                rows[Q * g + n, j, 0] = w[row_of[n, m]]
            for n in range(m + 1, FEATS):
                rows[Q * g + n, j, :] = w[row_of[m, n]]
    rows[DENSE_AT : DENSE_AT + DENSE, DENSE_SLOT, 0] = w[len(row_of) :]
    rows[DENSE_AT + DENSE :, DENSE_SLOT, :] = w[len(row_of) :, None]
    return rows


def part_signs():
    signs = np.ones((P, SLOTS), np.float32)
    for g in range(QUADS):
        for j in range(SLOT_COLS[g]):
            signs[Q * g + SLOTS * g + j + 1 : Q * (g + 1), j] = -1
    signs[DENSE_AT + DENSE :, DENSE_SLOT] = -1
    return signs


def build(nc, ids, small_ids, dense_t, tables, w1, signs, b1, w2, b2, w3, y):
    with ExitStack() as ctx:

        def sb(name, shape, dt=F32):
            return ctx.enter_context(nc.sbuf_tensor(name, shape, dt))

        def ps(name, shape):
            return ctx.enter_context(nc.psum_tensor(name, shape, F32))

        def sem(name):
            return ctx.enter_context(nc.semaphore(name))

        idt = [sb(f"idt{h}", [P, GATHERED], I32) for h in range(2)]
        rows = [sb(f"rows{h}", [P, GATHERED * P]) for h in range(2)]
        ident = sb("ident", [P, P])
        raw = [sb(f"raw{k}", [P, PIECE]) for k in range(RAWS)]
        raw += [rows[1][:, k * PIECE : (k + 1) * PIECE] for k in range(2)]
        table_hi = sb("table_hi", [P, ONEHOT, CHUNKS, P], F32R)
        table_lo = sb("table_lo", [P, ONEHOT, CHUNKS, P], F32R)
        small_f = sb("small_f", [ONEHOT, BATCH], F32R)
        pick = sb("pick", [ONEHOT, ONEHOT, ROWS], F32R)
        row_f = sb("row_f", [P, CHUNKS])
        mask = sb("mask", [P, MASKS, CHUNKS, PAIR], F32R)
        emb = sb("emb", [P, PAIR, Q])
        small_i = emb[0:ONEHOT, 0 : BATCH // Q, :].rearrange("t a b -> t (a b)").bitcast(I32)
        z = sb("z", [P, SLOTS, P])
        z_hi = sb("z_hi", [P, SLOTS, PAIR], F32R)
        z_lo = sb("z_lo", [P, SLOTS, PAIR], F32R)
        w1_sb = sb("w1_sb", [P, SLOTS, HID1], F32R)
        signs_sb = sb("signs_sb", [P, SLOTS])
        w2_hi = sb("w2_hi", [P, K1, HID2], F32R)
        w2_lo = sb("w2_lo", [P, K1, HID2], F32R)
        w3_sb = sb("w3_sb", [P, K2])
        b1_sb = sb("b1_sb", [P, K1])
        b2_sb = sb("b2_sb", [P, K2])
        h1_hi = sb("h1_hi", [P, K1, PAIR], F32R)
        h1_lo = sb("h1_lo", [P, K1, PAIR], F32R)
        h1 = raw[0][:, 0 : K1 * PAIR].rearrange("p (c b) -> p c b", c=K1)
        h2 = raw[1][:, 0 : K2 * PAIR].rearrange("p (c b) -> p c b", c=K2)
        pick_raw = z[0:ONEHOT, 0:ONEHOT, 0:ROWS]
        y_cols = sb("y_cols", [P, TILES])
        y_rows = rows[0][0:TILES, 0:P]
        row_i = y_cols[:, 0:CHUNKS].bitcast(I32)

        turned = [ps(f"turned{k}", [P, BANK]) for k in range(2)]
        gram = [ps(f"gram{k}", [P, FILL_BANKS, BANK]) for k in range(2)]
        mlp = ps("mlp", [P, JOB, PAIR])
        spread = ps("spread", [P, BANK_TABLES, PAIR])

        last1 = [spread[:, 0, :], turned[0][:, 0:PAIR], turned[1][:, 0:PAIR], gram[0][:, 0, 0:PAIR]]
        last2 = [gram[0][:, 1, 0:PAIR], gram[1][:, 0, 0:PAIR]]

        ids_in = [sem(f"ids_in{h}") for h in range(2)]
        rows_in = [[sem(f"rows_in{h}_{k}") for k in range(NG)] for h in range(2)]
        raw_in = [sem(f"raw_in{k}") for k in range(len(raw))]
        hi_cut = sem("hi_cut")
        lo_cut = sem("lo_cut")
        dense_in = sem("dense_in")
        small_ids_in = sem("small_ids_in")
        small_ids_cast = sem("small_ids_cast")
        small_in = sem("small_in")
        signs_in = sem("signs_in")
        emb_zeroed = sem("emb_zeroed")
        ident_made = sem("ident_made")
        pick_made = sem("pick_made")
        row_made = sem("row_made")
        consts_made = sem("consts_made")
        spread_full = sem("spread_full")
        mask_made = sem("mask_made")
        turned_full = sem("turned_full")
        turned_out = sem("turned_out")
        gram_full = sem("gram_full")
        z_act = sem("z_act")
        z_dve = sem("z_dve")
        z_hi_made = sem("z_hi_made")
        z_lo_made = sem("z_lo_made")
        h1_full = sem("h1_full")
        h1_hi_made = sem("h1_hi_made")
        h1_read = sem("h1_read")
        h1_lo_made = sem("h1_lo_made")
        h2_full = sem("h2_full")
        h2_out = sem("h2_out")
        y_full = sem("y_full")
        y_out = sem("y_out")
        y_turned = sem("y_turned")
        y_rows_made = sem("y_rows_made")
        y_stored = sem("y_stored")
        pool_marks = sem("pool_marks")
        sp_marks = sem("sp_marks")
        pe_marks = sem("pe_marks")

        def tile_of(i, h):
            return 2 * i + h

        def turned_by(i, job):
            return NJ * i + JOBS.index(job) + 1

        table_pieces = [
            (
                lambda r, k=k: r[0:ROWS, :].rearrange("p (c d) -> p c d", c=CHUNKS),
                tables[GATHERED + k].rearrange("(p c) d -> p c d", c=CHUNKS),
                table_hi[0:ROWS, k],
                table_lo[0:ROWS, k],
            )
            for k in range(ONEHOT)
        ]
        w1_pieces = [
            (lambda r: r[:, :].rearrange("p (k o) -> p k o", k=2), w1[:, j], w1_sb[:, j], None) for j in range(SLOTS)
        ]
        w2_pieces = [
            (
                lambda r: r[:, :].rearrange("p (k n) -> p k n", k=K1),
                w2.rearrange("(k p) n -> p k n", p=P),
                w2_hi[:, :, :],
                w2_lo[:, :, :],
            )
        ]
        pieces = table_pieces + w1_pieces + w2_pieces

        W2_PIECE = PIECES - 1
        assert len(pieces) == PIECES

        def before_in_place(n):
            same = [k for k in range(n) if PLACES[k] == PLACES[n]]
            return len(same), same[-1] + 1 if same else 0

        block = ctx.enter_context(nc.Block())

        @block.sync
        def _(sp):
            def load_ids(i, h, first):
                at = tile_of(i, h) * P if first else sp.snap(tile_of(i, h) * P)
                if not first:
                    for k, (_, n) in enumerate(GROUPS):
                        sp.wait_ge(rows_in[h][k], sp.snap(16 * n * i))
                        sp.sem_inc(sp_marks, 1)
                sp.dma_start(idt[h][:, :], ids[bass.ds(at, P), 0:GATHERED]).then_inc(ids_in[h], 16)

            def load_dense(i, h, first):
                at = tile_of(i, h) * P if first else sp.snap(tile_of(i, h) * P)
                if not (first and h == 0):
                    sp.wait_ge(z_lo_made, tile_of(i, h) if first else sp.snap(tile_of(i, h)))
                    sp.sem_inc(sp_marks, 1)
                sp.dma_start(
                    z[DENSE_AT:P, DENSE_SLOT, :], dense_t[:, bass.ds(at, P)]
                ).then_inc(dense_in, 16)

            def load_pieces(which):
                for n in which:
                    as_loaded, source, _, _ = pieces[n]
                    _, cut = before_in_place(n)
                    if cut:
                        sp.wait_ge(lo_cut, cut)
                    sp.dma_start(as_loaded(raw[PLACES[n]]), source).then_inc(raw_in[PLACES[n]], 16)

            load_ids(0, 0, True)
            load_ids(0, 1, True)
            sp.dma_start(small_i, small_ids).then_inc(small_ids_in, 16)
            load_pieces(range(ONEHOT))
            load_dense(0, 0, True)
            sp.dma_start(signs_sb[:, :], signs).then_inc(signs_in, 16)
            sp.dma_start(w3_sb[:, :], w3).then_inc(small_in, 16)
            sp.dma_start(b1_sb[:, :], b1).then_inc(small_in, 16)
            sp.dma_start(b2_sb[:, :], b2).then_inc(small_in, 16)
            load_pieces(range(7, 10))
            load_ids(1, 0, False)
            load_pieces([10, 11])
            load_ids(1, 1, False)
            load_pieces([12])
            load_dense(0, 1, True)
            load_pieces([13, W2_PIECE])
            load_dense(1, 0, False)
            with sp.Fori(2, TURNS) as i:
                load_ids(i, 0, False)
                load_ids(i, 1, False)
                load_dense(i - 1, 1, False)
                load_dense(i, 0, False)
            load_dense(TURNS - 1, 1, False)
            sp.wait_ge(y_rows_made, 1)
            sp.dma_start(y, y_rows[:, :]).then_inc(y_stored, 16)
            sp.wait_ge(y_stored, 16)

        @block.gpsimd
        def _(pool):
            def gather(i, h, first):
                pool.wait_ge(ids_in[h], 16 * (i + 1))
                if first and h == 1:
                    pool.wait_ge(lo_cut, 4)
                for k, (f0, n) in enumerate(GROUPS):
                    if not first:
                        pool.wait_ge(turned_full, turned_by(i - 1, ("T", h, k)))
                        pool.sem_inc(pool_marks, 1)
                    for f in range(f0, f0 + n):
                        pool.indirect_dma_start(
                            rows[h][:, f * P : (f + 1) * P],
                            None,
                            tables[f],
                            bass.IndirectOffsetOnAxis(ap=idt[h][:, f : f + 1], axis=0),
                        ).then_inc(rows_in[h][k], 16)

            pool.memset(pick_raw, 0.0).then_inc(pick_made, 1)
            pool.iota(row_i[:, :], pattern=[[1, CHUNKS]], base=0, channel_multiplier=CHUNKS).then_inc(row_made, 1)
            pool.wait_ge(pick_made, 1)
            pool.affine_select(
                out=pick_raw, in_=pick_raw, compare_op=ALU.not_equal, fill=1.0,
                base=0, pattern=[[-1, ONEHOT], [0, ROWS]], channel_multiplier=1,
            ).then_inc(pick_made, 1)
            pool.memset(ident[:, :], 0.0).then_inc(ident_made, 1)
            pool.wait_ge(ident_made, 1)
            pool.affine_select(
                out=ident[:, :], in_=ident[:, :], compare_op=ALU.not_equal, fill=1.0,
                base=0, pattern=[[-1, P]], channel_multiplier=1,
            ).then_inc(ident_made, 1)

            def turn(i, first):
                gather(i, 0, first)
                gather(i, 1, first)

            turn(0, True)
            with pool.Fori(1, TURNS) as i:
                turn(i, False)

        def take_fill(engine, copy, i, h, q, places=range(QUADS)):
            engine.wait_ge(gram_full, FILLS * tile_of(i, h) + q + 1)
            full = gram[q % 2][:, :, 0 : GRAMS_BANK * BLOCK].rearrange("p k (g s m) -> p k g s m", s=QUADS, m=COLS)
            to = z[:, :, q * FILL_SAMPLES : (q + 1) * FILL_SAMPLES]
            to = to.rearrange("p j (k g s) -> p k g s j", k=FILL_BANKS, s=QUADS)
            for s in places:
                for g in range(QUADS):
                    m0, n_m = SLOTS * g, SLOT_COLS[g]
                    last = copy(
                        to[Q * g : Q * (g + 1), :, :, s, 0:n_m],
                        full[Q * s : Q * (s + 1), :, :, s, m0 : m0 + n_m],
                    )
            return last

        @block.scalar
        def _(act):
            def copy(out, in_):
                return act.activation(out, in_, ACT.Copy)

            def cut_hi(which):
                for n in which:
                    as_loaded, _, hi, _ = pieces[n]
                    loaded, _ = before_in_place(n)
                    act.wait_ge(raw_in[PLACES[n]], 16 * (loaded + 1))
                    whole = as_loaded(raw[PLACES[n]])
                    if ONEHOT <= n < W2_PIECE:
                        whole = whole[:, 0]
                    copy(hi, whole).then_inc(hi_cut, 1)

            def to_emb(i, first, jobs):
                for job in jobs:
                    bank = turned[JOBS.index(job) % 2]
                    act.wait_ge(turned_full, turned_by(i, job))
                    if job[0] == "T":
                        _, h, k = job
                        f0, n = GROUPS[k]
                        if k == 0 and not first:
                            act.wait_ge(gram_full, FILLS * (tile_of(i, h) - 1))
                        out = emb[:, h * P : (h + 1) * P, f0 : f0 + n]
                        copy(out, bank[:, 0 : n * P].rearrange("p (f b) -> p b f", b=P)).then_inc(turned_out, 1)
                    else:
                        tables_in = LOOKUPS[job[1]]
                        f, n = GATHERED + tables_in[0], len(tables_in)
                        if job[1] == 0 and not first:
                            act.wait_ge(gram_full, FILLS * tile_of(i, 0))
                        out = emb[:, :, f : f + n]
                        copy(out, bank[:, 0 : n * PAIR].rearrange("p (k b) -> p b k", b=PAIR)).then_inc(turned_out, 1)

            def fill(i, h, q, first=False):
                if q == 0 and not (first and h == 0):
                    act.wait_ge(z_lo_made, tile_of(i, h))
                take_fill(act, copy, i, h, q).then_inc(z_act, 1)

            def cut_z_hi(i, h):
                act.wait_ge(z_act, ACT_FILLS * (tile_of(i, h) + 1))
                act.wait_ge(z_dve, tile_of(i, h) + 1)
                act.wait_ge(dense_in, 16 * (tile_of(i, h) + 1))
                copy(z_hi[:, :, h * P : (h + 1) * P], z[:, :, :]).then_inc(z_hi_made, 1)

            def layer1(p, chunks, banks=(mlp[:, 0, :], mlp[:, 1, :])):
                act.wait_ge(h1_full, K1 * p + chunks[-1] + 1)
                for k, bank in zip(chunks, banks):
                    act.activation(h1_hi[:, k, :], bank, ACT.Relu, bias=b1_sb[:, k : k + 1]).then_inc(h1_hi_made, 1)

            def layer2(p, banks=(mlp[:, 0, :], mlp[:, 1, :])):
                act.wait_ge(h2_full, p + 1)
                for c in range(K2):
                    last = act.activation(h2[:, c, :], banks[c], ACT.Relu, bias=b2_sb[:, c : c + 1])
                last.then_inc(h2_out, 1)

            def layer3(p):
                act.wait_ge(y_full, p + 1)
                copy(y_cols[:, bass.ds(2 * p, 2)], mlp[:, 0, 0:2]).then_inc(y_out, 1)

            def turn(i, first=False, second=False, last=False):
                to_emb(i, first, JOBS[0:1])
                if first:
                    cut_hi([2, 3])
                else:
                    fill(i - 1, 1, 0)
                    fill(i - 1, 1, 1)
                to_emb(i, first, JOBS[1:2])
                if first:
                    cut_hi([4])
                else:
                    fill(i - 1, 1, 2)
                to_emb(i, first, JOBS[2:3])
                if first:
                    cut_hi([5])
                else:
                    cut_z_hi(i - 1, 1)
                if second:
                    cut_hi([12])
                to_emb(i, first, JOBS[3:5])
                if not first and not second:
                    layer3(i - 2)
                if first:
                    cut_hi([6])
                if second:
                    cut_hi([13])
                to_emb(i, first, JOBS[5:6])
                if first:
                    cut_hi([7])
                to_emb(i, first, JOBS[6:8])
                if first:
                    cut_hi([8])
                else:
                    layer1(i - 1, [0, 1])
                if second:
                    cut_hi([W2_PIECE])
                to_emb(i, first, JOBS[8:9])
                if first:
                    cut_hi([9])
                to_emb(i, first, JOBS[9:10])
                fill(i, 0, 0, first)
                fill(i, 0, 1, first)
                to_emb(i, first, JOBS[10:11])
                fill(i, 0, 2, first)
                if first:
                    cut_hi([10])
                to_emb(i, first, JOBS[11:12])
                if not first:
                    layer1(i - 1, [2, 3])
                to_emb(i, first, JOBS[12:])
                cut_z_hi(i, 0)
                if first:
                    cut_hi([11])
                if second:
                    act.wait_ge(lo_cut, PIECES)
                if not first and not last:
                    layer2(i - 1)

            cut_hi([0, 1])
            act.wait_ge(emb_zeroed, 1)
            turn(0, first=True)
            act.wait_ge(small_in, 48)
            turn(1, second=True)
            with act.Fori(2, TURNS - 1) as i:
                turn(i)
            turn(TURNS - 1, last=True)
            for q in range(ACT_FILLS):
                fill(TURNS - 1, 1, q)
            act.wait_ge(dense_in, 16 * TILES)
            act.wait_ge(z_act, ACT_FILLS * TILES)
            copy(z_hi[:, :, P : P + LAST_SAMPLES], z[:, :, 0:LAST_SAMPLES]).then_inc(z_hi_made, 1)
            take_fill(act, copy, TURNS - 1, 1, FILLS - 1, places=range(QUADS // 2)).then_inc(z_act, 1)
            act.wait_ge(z_act, ACT_FILLS * TILES + 1)
            act.wait_ge(z_dve, TILES)
            copy(z_hi[:, :, P + LAST_SAMPLES :], z[:, :, LAST_SAMPLES:P]).then_inc(z_hi_made, 1)
            layer2(TURNS - 2)
            for k in range(K1):
                layer1(TURNS - 1, [k], last1[k:])
            layer3(TURNS - 2)
            layer2(TURNS - 1, banks=last2)
            layer3(TURNS - 1)
            act.wait_ge(y_turned, 1)
            copy(y_rows[:, :], mlp[0:TILES, 0, 0:P]).then_inc(y_rows_made, 1)

        @block.vector
        def _(dve):
            def copy(out, in_):
                return dve.tensor_copy(out, in_)

            def cut_lo(which):
                for n in which:
                    as_loaded, _, hi, lo = pieces[n]
                    dve.wait_ge(hi_cut, n + 1)
                    whole = as_loaded(raw[PLACES[n]])
                    if ONEHOT <= n < W2_PIECE:
                        j = n - ONEHOT
                        dve.scalar_tensor_tensor(
                            hi, hi.bitcast(F32), signs_sb[:, j : j + 1], whole[:, 1], ALU.mult, ALU.add
                        ).then_inc(lo_cut, 1)
                    else:
                        dve.tensor_tensor(lo, whole, hi.bitcast(F32), ALU.subtract).then_inc(lo_cut, 1)

            def one_hot(i, k, used_in=None):
                if used_in is not None:
                    before = max(b for b in range(-1, ONEHOT) if b % MASKS == k % MASKS and (b < k or k < MASKS))
                    dve.wait_ge(turned_full, turned_by(used_in, ("O", before // BANK_TABLES)))
                dve.wait_ge(spread_full, len(LOOKUPS) * i + k // BANK_TABLES + 1)
                for c in range(CHUNKS):
                    last = dve.tensor_scalar(
                        mask[0:ROWS, k % MASKS, c, :], spread[0:ROWS, k % BANK_TABLES, :], row_f[0:ROWS, c : c + 1], None,
                        ALU.is_equal,
                    )
                last.then_inc(mask_made, 1)

            def fill(i, h, q, first=False):
                if not (first and h == 0):
                    dve.wait_ge(z_lo_made, tile_of(i, h))
                take_fill(dve, copy, i, h, q).then_inc(z_dve, 1)

            def cut_z_lo(i, h):
                dve.wait_ge(z_hi_made, tile_of(i, h) + 1)
                tile = slice(h * P, (h + 1) * P)
                dve.tensor_tensor(z_lo[:, :, tile], z[:, :, :], z_hi[:, :, tile].bitcast(F32), ALU.subtract).then_inc(
                    z_lo_made, 1
                )

            def layer1(p, chunks, banks=(mlp[:, 0, :], mlp[:, 1, :])):
                dve.wait_ge(h1_hi_made, K1 * p + chunks[-1] + 1)
                for k, bank in zip(chunks, banks):
                    dve.tensor_scalar(h1[:, k, :], bank, b1_sb[:, k : k + 1], 0.0, ALU.add, ALU.max).then_inc(
                        h1_read, 1
                    )
                for k in chunks:
                    dve.wait_ge(h1_read, K1 * p + k + 1)
                    dve.tensor_tensor(h1_lo[:, k, :], h1[:, k, :], h1_hi[:, k, :].bitcast(F32), ALU.subtract).then_inc(
                        h1_lo_made, 1
                    )

            def turn(i, first=False, second=False, last=False):
                if first:
                    for k in range(MASKS):
                        cut_lo([k + 1])
                        one_hot(0, k)
                    cut_lo([5])
                else:
                    one_hot(i, 3, used_in=i - 1)
                    fill(i - 1, 1, 3)
                    cut_z_lo(i - 1, 1)
                if second:
                    cut_lo([12])
                one_hot(i, 4, used_in=i)
                if first:
                    cut_lo([6])
                if second:
                    cut_lo([13])
                one_hot(i, 5, used_in=i)
                if first:
                    dve.wait_ge(signs_in, 16)
                    cut_lo([7])
                one_hot(i, 6, used_in=i)
                if first:
                    cut_lo([8])
                else:
                    layer1(i - 1, [0, 1])
                if second:
                    cut_lo([W2_PIECE])
                if not last:
                    one_hot(i + 1, 0, used_in=i)
                if first:
                    cut_lo([9])
                if not last:
                    one_hot(i + 1, 1, used_in=i)
                if first:
                    cut_lo([10])
                elif not last:
                    layer1(i - 1, [2, 3])
                fill(i, 0, 3, first)
                cut_z_lo(i, 0)
                if last:
                    layer1(i - 1, [2, 3])
                if first:
                    cut_lo([11])
                if not last:
                    one_hot(i + 1, 2, used_in=i)

            dve.wait_ge(pick_made, 2)
            copy(pick[:, :, :], pick_raw).then_inc(consts_made, 1)
            dve.wait_ge(row_made, 1)
            copy(row_f[:, :], row_i[:, :]).then_inc(consts_made, 1)
            dve.wait_ge(small_ids_in, 16)
            copy(small_f[:, :], small_i).then_inc(small_ids_cast, 1)
            dve.wait_ge(consts_made, 2)
            dve.wait_ge(small_ids_cast, 1)
            dve.memset(emb[:, :, FEATS:Q], 0.0).then_inc(emb_zeroed, 1)
            cut_lo([0])
            turn(0, first=True)
            dve.wait_ge(small_in, 48)
            turn(1, second=True)
            with dve.Fori(2, TURNS - 1) as i:
                turn(i)
            turn(TURNS - 1, last=True)
            take_fill(dve, copy, TURNS - 1, 1, FILLS - 1, places=range(QUADS // 2, QUADS)).then_inc(z_dve, 1)
            for n, cut in enumerate((slice(0, LAST_SAMPLES), slice(LAST_SAMPLES, P))):
                dve.wait_ge(z_hi_made, TILES + n)
                part = slice(P + cut.start, P + cut.stop)
                dve.tensor_tensor(z_lo[:, :, part], z[:, :, cut], z_hi[:, :, part].bitcast(F32), ALU.subtract).then_inc(
                    z_lo_made, 1
                )
            for k in range(K1):
                layer1(TURNS - 1, [k], last1[k:])

        @block.tensor
        def _(pe):
            def transposes(i, h, k, first):
                f0, n = GROUPS[k]
                bank = turned_job(i, ("T", h, k), first)
                pe.wait_ge(rows_in[h][k], 16 * n * (i + 1))
                for c in range(n):
                    last = pe.transpose(
                        bank[:, c * P : (c + 1) * P], rows[h][:, (f0 + c) * P : (f0 + c + 1) * P], ident[:, :]
                    )
                last.then_inc(turned_full, 1)

            def turned_job(i, job, first):
                at = JOBS.index(job)
                if not (first and at < 2):
                    pe.wait_ge(turned_out, NJ * i + at - 1)
                return turned[at % 2]

            def lookup(i, k, first):
                g, place = divmod(k, BANK_TABLES)
                bank = turned_job(i, ("O", g), first) if place == 0 else turned[JOBS.index(("O", g)) % 2]
                if first:
                    pe.wait_ge(lo_cut, k + 1)
                pe.wait_ge(mask_made, ONEHOT * i + k + 1)
                for c in range(CHUNKS):
                    for part in (table_hi, table_lo):
                        last = pe.matmul(
                            bank[:, place * PAIR : (place + 1) * PAIR],
                            part[0:ROWS, k, c, :],
                            mask[0:ROWS, k % MASKS, c, :],
                            start=c == 0 and part is table_hi,
                            stop=c == CHUNKS - 1 and part is table_lo,
                        )
                if k == LOOKUPS[g][-1]:
                    last.then_inc(turned_full, 1)

            def spread_ids(i, g, first=False):
                if not first:
                    pe.wait_ge(mask_made, ONEHOT * i + LOOKUPS[g][0])
                    pe.sem_inc(pe_marks, 1)
                for place, k in enumerate(LOOKUPS[g]):
                    last = pe.matmul(
                        spread[0:ROWS, place, :], pick[:, k, :], small_f[:, bass.ds(i * PAIR, PAIR)], start=True, stop=True
                    )
                last.then_inc(spread_full, 1)

            def fill(i, h, q, first=False):
                if q == 0:
                    pe.wait_ge(turned_out, turned_by(i, ("O", len(LOOKUPS) - 1) if h == 0 else ("T", 1, NG - 1)))
                if not (first and h == 0 and q < 2):
                    if q == 1:
                        pe.wait_ge(z_dve, tile_of(i, h))
                    else:
                        pe.wait_ge(z_act, ACT_FILLS * tile_of(i, h) + max(q - 1, 0))
                for n in range(GRAMS_FILL):
                    b0 = h * P + q * FILL_SAMPLES + n * QUADS
                    at = n % GRAMS_BANK * BLOCK
                    last = pe.matmul(
                        gram[q % 2][:, n // GRAMS_BANK, at : at + BLOCK],
                        emb[:, b0 : b0 + QUADS, :],
                        emb[:, b0 : b0 + QUADS, 0:FEATS],
                        start=True,
                        stop=True,
                    )
                last.then_inc(gram_full, 1)

            def layer1(p, c, first=False, bank=None):
                place = c % JOB
                more = 0 if bank is None else 1
                if c == 0:
                    if not more and not first:
                        pe.wait_ge(y_out, p)
                    pe.wait_ge(z_hi_made, 2 * (p + 1) + more)
                elif place == 0 and not more:
                    pe.wait_ge(h1_read, K1 * p + JOB)
                for part in (z_hi, z_lo):
                    if c == 0 and part is z_lo:
                        pe.wait_ge(z_lo_made, 2 * (p + 1) + more)
                    for j in range(SLOTS):
                        last = pe.matmul(
                            bank if more else mlp[:, place, :],
                            w1_sb[:, j, c * P : (c + 1) * P],
                            part[:, j, :],
                            start=j == 0 and part is z_hi,
                            stop=j == SLOTS - 1 and part is z_lo,
                        )
                last.then_inc(h1_full, 1)

            def layer2(p):
                pe.wait_ge(h1_lo_made, K1 * (p + 1))
                for c in range(K2):
                    cols = slice(c * P, (c + 1) * P)
                    for k in range(K1):
                        for left, right in ((w2_hi, h1_hi), (w2_lo, h1_hi), (w2_hi, h1_lo)):
                            last = pe.matmul(
                                mlp[:, c, :],
                                left[:, k, cols],
                                right[:, k, :],
                                start=k == 0 and left is w2_hi and right is h1_hi,
                                stop=k == K1 - 1 and right is h1_lo,
                            )
                last.then_inc(h2_full, 1)

            def layer2_last(p):
                for k in range(K1):
                    if k == JOB:
                        layer3(p - 1)
                    pe.wait_ge(h1_lo_made, K1 * p + k + 1)
                    for c, bank in enumerate(last2):
                        for left, right in ((w2_hi, h1_hi), (w2_lo, h1_hi), (w2_hi, h1_lo)):
                            last = pe.matmul(
                                bank,
                                left[:, k, c * P : (c + 1) * P],
                                right[:, k, :],
                                start=k == 0 and left is w2_hi and right is h1_hi,
                                stop=k == K1 - 1 and right is h1_lo,
                            )
                last.then_inc(h2_full, 1)

            def layer3(p):
                pe.wait_ge(h2_out, p + 1)
                for h in range(2):
                    for k in range(K2):
                        last = pe.matmul(
                            mlp[:, 0, h : h + 1], h2[:, k, h * P : (h + 1) * P], w3_sb[:, k : k + 1],
                            start=k == 0, stop=k == K2 - 1,
                        )
                last.then_inc(y_full, 1)

            def turn(i, first=False, second=False, last=False):
                transposes(i, 0, 0, first)
                if not first:
                    fill(i - 1, 1, 0)
                    fill(i - 1, 1, 1)
                transposes(i, 0, 1, first)
                if first:
                    spread_ids(0, 1)
                if not first:
                    fill(i - 1, 1, 2)
                    fill(i - 1, 1, 3)
                transposes(i, 0, 2, first)
                lookup(i, 0, first)
                if not first:
                    spread_ids(i, 2)
                lookup(i, 1, first)
                if first:
                    spread_ids(i, 2)
                transposes(i, 0, 3, first)
                if not first and not second:
                    layer3(i - 2)
                lookup(i, 2, first)
                lookup(i, 3, first)
                if second:
                    pe.wait_ge(lo_cut, W2_PIECE)
                if not first:
                    layer1(i - 1, 0, second)
                transposes(i, 0, 4, first)
                if not first:
                    spread_ids(i, 3)
                lookup(i, 4, first)
                if first:
                    spread_ids(i, 3)
                lookup(i, 5, first)
                if not first:
                    layer1(i - 1, 1)
                lookup(i, 6, first)
                if not last:
                    spread_ids(i + 1, 0)
                transposes(i, 1, 0, first)
                fill(i, 0, 0, first)
                fill(i, 0, 1, first)
                transposes(i, 1, 1, first)
                if not first:
                    layer1(i - 1, 2)
                fill(i, 0, 2, first)
                transposes(i, 1, 2, first)
                if last:
                    fill(i, 0, 3)
                if not first:
                    layer1(i - 1, 3)
                if not last:
                    spread_ids(i + 1, 1)
                    fill(i, 0, 3, first)
                transposes(i, 1, 3, first)
                transposes(i, 1, 4, first)
                if second:
                    pe.wait_ge(lo_cut, PIECES)
                    pe.wait_ge(small_in, 48)
                if not first and not last:
                    layer2(i - 1)

            pe.wait_ge(consts_made, 2)
            pe.wait_ge(small_ids_cast, 1)
            spread_ids(0, 0, first=True)
            pe.wait_ge(ident_made, 2)
            pe.wait_ge(emb_zeroed, 1)
            turn(0, first=True)
            turn(1, second=True)
            with pe.Fori(2, TURNS - 1) as i:
                turn(i)
            turn(TURNS - 1, last=True)
            for q in range(FILLS):
                fill(TURNS - 1, 1, q)
            layer2(TURNS - 2)
            for c in range(K1):
                layer1(TURNS - 1, c, bank=last1[c])
            layer2_last(TURNS - 1)
            layer3(TURNS - 1)
            pe.wait_ge(y_out, TURNS)
            pe.transpose(mlp[0:TILES, 0, 0:P], y_cols[:, :], ident[:, :]).then_inc(y_turned, 1)


def kernel(**inputs):
    import numpy as _np
    import concourse.bacc as _bacc
    from concourse import mybir as _mybir
    from concourse.bass_utils import run_bass_kernel_spmd as _run

    nc = _bacc.Bacc("TRN2", target_bir_lowering=False, num_devices=1)
    arrays = {}

    def put(name, a):
        a = _np.ascontiguousarray(a)
        arrays[name] = a
        return nc.dram_tensor(name, a.shape, _mybir.dt.from_np(a.dtype), kind="ExternalInput").ap()

    get = lambda name: _np.asarray(inputs[name])
    y = nc.dram_tensor("y", (TILES, P), F32, kind="ExternalOutput").ap()
    build(
        nc,
        ids=put("ids", get("ids")),
        small_ids=put("small_ids", get("ids")[:, GATHERED:].T),
        dense_t=put("dense_t", _np.tile(get("dense_ctx").T, (2, 1))),
        tables=[put(f"tbl_{f}", get(f"tbl_{f}")) for f in range(FEATS)],
        w1=put("w1", lay_w1(get("W_top1"))),
        signs=put("signs", part_signs()),
        b1=put("b1", get("b_top1").reshape(K1, P).T),
        w2=put("w2", get("W_top2")),
        b2=put("b2", get("b_top2").reshape(K2, P).T),
        w3=put("w3", get("W_top3").reshape(K2, P).T),
        y=y,
    )
    r = _run(nc, [arrays], core_ids=[0])
    return r.results[0]["y"].reshape(BATCH, 1)
```
